# Optimizing a Trainium2 kernel written in Bass

```python
import numpy as np
import jax
import jax.numpy as jnp

def _softmax(x, axis=-1):
    return jax.nn.softmax(x, axis=axis)

def _gelu(x):
    return jax.nn.gelu(x, approximate=True)

def _silu(x):
    return jax.nn.silu(x)

def _sigmoid(x):
    return jax.nn.sigmoid(x)

def _layernorm(x, axis=-1, eps=1e-05):
    m = jnp.mean(x, axis=axis, keepdims=True)
    v = jnp.var(x, axis=axis, keepdims=True)
    return (x - m) / jnp.sqrt(v + eps)

def _scatter_add(tgt, idx, src, axis=0):
    return tgt.at[idx].add(src)

def _segment_sum(src, seg, n):
    return jax.ops.segment_sum(src, seg, n)
kernel_name = 'mk_seq_postln_d1_jaxref_r4_463f19'

def setup_inputs(seed: int=0):
    np.random.seed(seed)
    _w = jnp.asarray

    def _L0_attn_setup():
        import jax, jax.numpy as jnp
        import numpy as np
        N_HEADS = 16
        EPS = 0.0001

        def _cosformer(x, Wq, bq, Wk, bk, Wv, bv, Wo, bo):
            B, L, E = x.shape
            H = N_HEADS
            hd = E // H
            q = jax.nn.relu(jnp.einsum('ble,fe->blf', x, Wq) + bq)
            k = jax.nn.relu(jnp.einsum('ble,fe->blf', x, Wk) + bk)
            v = jnp.einsum('ble,fe->blf', x, Wv) + bv

            def split_heads(t):
                return t.reshape(B, L, H, hd).transpose(0, 2, 1, 3).reshape(B * H, L, hd)
            q, k, v = (split_heads(q), split_heads(k), split_heads(v))
            m = L
            idx = np.pi / 2 * jnp.arange(1, m + 1, dtype=jnp.float32) / m
            sin = jnp.sin(idx)[None, :, None]
            cos = jnp.cos(idx)[None, :, None]
            q_ = jnp.concatenate([q * sin, q * cos], axis=-1)
            k_ = jnp.concatenate([k * sin, k * cos], axis=-1)
            kv = jnp.einsum('nld,nlm->ndm', k_, v)
            z = 1.0 / jnp.maximum(jnp.einsum('nld,nd->nl', q_, k_.sum(axis=1)), EPS)
            attn = jnp.einsum('nld,ndm->nlm', q_, kv) * z[:, :, None]
            out = attn.reshape(B, H, L, hd).transpose(0, 2, 1, 3).reshape(B, L, E)
            return jnp.einsum('ble,fe->blf', out, Wo) + bo
        key = jax.random.key(seed)
        ks = jax.random.split(key, 9)
        B, L, E = (4, 1024, 256)
        s = 1.0 / np.sqrt(E)
        return {'x': jax.random.normal(ks[0], (B, L, E), dtype=jnp.float32), 'Wq': jax.random.normal(ks[1], (E, E), dtype=jnp.float32) * s, 'bq': jax.random.normal(ks[2], (E,), dtype=jnp.float32) * 0.01, 'Wk': jax.random.normal(ks[3], (E, E), dtype=jnp.float32) * s, 'bk': jax.random.normal(ks[4], (E,), dtype=jnp.float32) * 0.01, 'Wv': jax.random.normal(ks[5], (E, E), dtype=jnp.float32) * s, 'bv': jax.random.normal(ks[6], (E,), dtype=jnp.float32) * 0.01, 'Wo': jax.random.normal(ks[7], (E, E), dtype=jnp.float32) * s, 'bo': jax.random.normal(ks[8], (E,), dtype=jnp.float32) * 0.01}
    _L0_attn_in = _L0_attn_setup()

    def _L0_ffn_setup():
        import jax, jax.numpy as jnp
        import numpy as np
        B, S, H, E, K = (4, 512, 256, 8, 2)
        key = jax.random.key(seed)
        k0, k1, k2, k3 = jax.random.split(key, 4)
        x = jax.random.normal(k0, (B, S, H), dtype=jnp.float32)
        router_w = jax.random.normal(k1, (E, H), dtype=jnp.float32) * np.float32(1.0 / np.sqrt(H))
        xav1 = np.float32(np.sqrt(2.0 / (2 * H + H)))
        w1 = jax.random.normal(k2, (E, 2 * H, H), dtype=jnp.float32) * xav1
        w2 = jax.random.normal(k3, (E, H, 2 * H), dtype=jnp.float32) * xav1
        return {'x': x, 'router_w': router_w, 'w1': w1, 'w2': w2}
    _L0_ffn_in = _L0_ffn_setup()
    _d = {'L0_attn_x': _L0_attn_in['x'], 'L0_attn_Wq': _L0_attn_in['Wq'], 'L0_attn_bq': _L0_attn_in['bq'], 'L0_attn_Wk': _L0_attn_in['Wk'], 'L0_attn_bk': _L0_attn_in['bk'], 'L0_attn_Wv': _L0_attn_in['Wv'], 'L0_attn_bv': _L0_attn_in['bv'], 'L0_attn_Wo': _L0_attn_in['Wo'], 'L0_attn_bo': _L0_attn_in['bo'], 'L0_ffn_router_w': _L0_ffn_in['router_w'], 'L0_ffn_w1': _L0_ffn_in['w1'], 'L0_ffn_w2': _L0_ffn_in['w2']}
    _x0 = _d['L0_attn_x']
    _d['L0_attn_x'] = jax.random.normal(jax.random.fold_in(jax.random.key(seed), 1), (4, 2048, 256), dtype=_x0.dtype)
    del _x0
    return _d

def reference(L0_attn_x, L0_attn_Wq, L0_attn_bq, L0_attn_Wk, L0_attn_bk, L0_attn_Wv, L0_attn_bv, L0_attn_Wo, L0_attn_bo, L0_ffn_router_w, L0_ffn_w1, L0_ffn_w2):

    def _L0_attn_ref(x, Wq, bq, Wk, bk, Wv, bv, Wo, bo):
        import jax, jax.numpy as jnp
        import numpy as np
        N_HEADS = 16
        EPS = 0.0001

        def _cosformer(x, Wq, bq, Wk, bk, Wv, bv, Wo, bo):
            B, L, E = x.shape
            H = N_HEADS
            hd = E // H
            q = jax.nn.relu(jnp.einsum('ble,fe->blf', x, Wq) + bq)
            k = jax.nn.relu(jnp.einsum('ble,fe->blf', x, Wk) + bk)
            v = jnp.einsum('ble,fe->blf', x, Wv) + bv

            def split_heads(t):
                return t.reshape(B, L, H, hd).transpose(0, 2, 1, 3).reshape(B * H, L, hd)
            q, k, v = (split_heads(q), split_heads(k), split_heads(v))
            m = L
            idx = np.pi / 2 * jnp.arange(1, m + 1, dtype=jnp.float32) / m
            sin = jnp.sin(idx)[None, :, None]
            cos = jnp.cos(idx)[None, :, None]
            q_ = jnp.concatenate([q * sin, q * cos], axis=-1)
            k_ = jnp.concatenate([k * sin, k * cos], axis=-1)
            kv = jnp.einsum('nld,nlm->ndm', k_, v)
            z = 1.0 / jnp.maximum(jnp.einsum('nld,nd->nl', q_, k_.sum(axis=1)), EPS)
            attn = jnp.einsum('nld,ndm->nlm', q_, kv) * z[:, :, None]
            out = attn.reshape(B, H, L, hd).transpose(0, 2, 1, 3).reshape(B, L, E)
            return jnp.einsum('ble,fe->blf', out, Wo) + bo
        return _cosformer(x, Wq, bq, Wk, bk, Wv, bv, Wo, bo)

    def _L0_ffn_ref(x, router_w, w1, w2):
        import jax, jax.numpy as jnp
        import numpy as np
        B, S, H, E, K = (4, 512, 256, 8, 2)
        bsz, seq, hidden = x.shape
        n_experts = w1.shape[0]
        tokens = x.reshape(-1, hidden)
        T = tokens.shape[0]
        logits = tokens @ router_w.T
        topv, topi = jax.lax.top_k(logits, K)
        w = jax.nn.softmax(topv, axis=-1).astype(tokens.dtype)
        gate = jnp.zeros((T, n_experts), tokens.dtype).at[jnp.arange(T)[:, None], topi].add(w)
        out = jnp.zeros_like(tokens)
        for e in range(n_experts):
            h = jax.nn.gelu(tokens @ w1[e].T, approximate=False)
            y = h @ w2[e].T
            out = out + gate[:, e:e + 1] * y
        return out.reshape(bsz, seq, hidden)
    x = L0_attn_x
    x = _layernorm(x + _L0_attn_ref(x, L0_attn_Wq, L0_attn_bq, L0_attn_Wk, L0_attn_bk, L0_attn_Wv, L0_attn_bv, L0_attn_Wo, L0_attn_bo), axis=-1)
    x = _layernorm(x + _L0_ffn_ref(x, L0_ffn_router_w, L0_ffn_w1, L0_ffn_w2), axis=-1)
    return x

_drawn_inputs = setup_inputs


def setup_inputs(seed=0):
    import zlib

    import numpy as np

    out = dict(_drawn_inputs(seed))
    spreads = {}
    factors = {'L0_attn_bq': 26.704, 'L0_attn_bk': 32.512}
    for name, (base, spread) in spreads.items():
        noise = np.random.default_rng([zlib.crc32(name.encode()), seed]).standard_normal(out[name].shape)
        drawn = base * np.exp(spread * noise) if base else spread * noise
        out[name] = jnp.asarray(drawn.astype(out[name].dtype))
    for name, factor in factors.items():
        out[name] = (out[name] * factor).astype(out[name].dtype)
    return out
```

```python
from contextlib import ExitStack

import numpy as np
import concourse.bass as bass
from concourse import mybir

F32 = mybir.dt.float32
F32R = mybir.dt.float32r
BF16 = mybir.dt.bfloat16
U32 = mybir.dt.uint32
I32 = mybir.dt.int32
ALU = mybir.AluOpType
ACT = mybir.ActivationFunctionType
AX_X = mybir.AxisListType.X
ENG = mybir.EngineType

P = 128
B, L, D = 4, 2048, 256
H, HD = 16, 16
E, F, TOPK = 8, 512, 2
T = B * L
KD = D // P
KF = F // P
HH = H // KD
PAIR = 2 * P
NPAIR = T // PAIR
PB = L // PAIR
LAG = PB + 1
NT_B = L // P
VW = P + 1
NW = P + HH
ATT_EPS = 1e-4
LN_EPS = 1e-5

ROW = D + 4
C_DST, C_GATE, C_FLAG = D, D + 1, D + 2
REGION = T + P
STEPS = TOPK * T // P + E
NO_ROW = 1 << 24

CO = {}
NCONST = 0
for _name, _n in (("ident", P), ("block", P), ("heads", HH), ("experts", E), ("region", E), ("sin", NT_B),
                  ("cos", NT_B), ("dst", 2 * TOPK), ("step", 2), ("before", P),
                  ("upto", E * E)):
    CO[_name] = (NCONST, NCONST + _n)
    NCONST += _n


def shape_constants():
    p = np.arange(P)
    c = np.zeros((P, NCONST), np.float32)

    def put(name, a):
        c[:, CO[name][0]:CO[name][1]] = a

    put("ident", p[:, None] == p[None, :])
    put("block", p[:, None] // HD == p[None, :] // HD)
    put("heads", p[:, None] // HD == np.arange(HH)[None, :])
    put("experts", np.arange(E)[None, :])
    put("region", (np.arange(E) * REGION)[None, :])
    place = (np.float32(np.pi / 2) * np.arange(1, L + 1, dtype=np.float32) / np.float32(L)).astype(np.float32)
    place = place.reshape(NT_B, P).T
    put("sin", np.sin(place))
    put("cos", np.cos(place))
    put("dst", (TOPK * (p[:, None, None] + P * np.arange(2)[None, :, None])
                + np.arange(TOPK)[None, None, :]).reshape(P, 2 * TOPK))
    put("step", p[:, None] + P * np.arange(2)[None, :])
    put("before", p[:, None] < p[None, :])
    put("upto", (np.arange(E)[None, :] <= np.arange(E)[:, None]).reshape(1, E * E))
    return c


def build(nc, x, xT, WqT, bq, WkT, bk, WvT, bv, WoT, bo, rwT, w1T, w2T, consts, out):
    ctx = ExitStack()
    first = ExitStack()
    ex = nc.dram_tensor("expert_rows", (E * REGION + P, ROW), F32).ap()
    yd = nc.dram_tensor("token_rows", (TOPK * T, D), F32).ap()
    with ctx:
        def sb(name, shape, dt=F32, stack=ctx):
            return stack.enter_context(nc.sbuf_tensor(name, [P] + shape, dt))

        def sem(name):
            return ctx.enter_context(nc.semaphore(name))

        PS = ctx.enter_context(nc.psum_tensor("PS", [P, 8, 512], F32))
        bKV, bST, bN, bA, bQ, bC = 0, 1, 3, 5, 6, 7
        gX, gH, gT, gY = 0, 2, 4, 6

        cst = sb("cst", [NCONST])
        half_neg = sb("half_neg", [4])
        ones_bf = sb("ones_bf", [P], BF16)
        before_bf = sb("before_bf", [P], BF16)
        cum = sb("cum", [2, E], BF16)
        tail = sb("tail", [ROW])
        cnt = sb("cnt", [E])
        tails_f = sb("tails_f", [E])
        tails_i = sb("tails_i", [E], I32)
        cnt_i = sb("cnt_i", [E], I32)
        tiles_i = sb("tiles_i", [E], I32)
        tiles_f = sb("tiles_f", [E])
        upto = sb("upto", [E, E])
        ends = sb("ends", [E])
        jump = sb("jump", [E])
        past = sb("past", [2, E])
        past_j = sb("past_j", [2, E])
        sums = sb("sums", [2, 2])
        table = sb("table", [2, 2])
        steps = sb("steps", [2 * P], I32)

        def const(name):
            return cst[:, CO[name][0]:CO[name][1]]

        WE = 2 * KD * F
        HALF = KD * F
        LATE = 2
        EARLY = E - LATE
        raws = ExitStack()
        rwk, rwv, rwq, rwo = (sb(n, [KD, D], F32, raws) for n in ("raw_wk", "raw_wv", "raw_wq", "raw_wo"))
        raws.close()
        whole = ExitStack()
        w = sb("w", [E, 2, WE], F32R, whole)
        whole.close()
        sb("w_early_place", [EARLY, 2, WE], F32, first)
        wkv = sb("wkv", [2, KD, 2 * D], F32R, first)
        wq = sb("wq", [2, KD, D], F32R, first)
        wo = sb("wo", [2, KD, D], F32R, first)
        rw = sb("rw", [KD, E], F32, first)
        bkv = sb("bkv", [2 * KD, P], F32, first)
        bqc = sb("bqc", [KD], F32, first)
        bob = sb("bob", [D], F32, first)
        wraw = sb("wraw", [2, HALF], F32, first)
        xraw = sb("xraw", [2, KD, PAIR], F32, first)
        xs = sb("xs", [2, 2, KD, PAIR], F32R, first)
        kvb = sb("kvb", [2, 2 * KD, VW], F32, first)
        kr = sb("kr", [2, KD, P], F32, first)
        vs = sb("vs", [2, KD, 2, VW], F32, first)
        q32 = sb("q32", [PB, KD, PAIR], F32, first)
        qs = sb("qs", [2, KD, PAIR], F32R, first)
        st32 = sb("st32", [KD, 2, NW], F32, first)
        sts = sb("sts", [2, KD, 2, NW], F32R, first)
        tcos = sb("tcos", [KD, NW], F32, first)
        o = sb("o", [2, KD, NW], F32, first)
        den = sb("den", [2 * KD, HH], F32, first)
        zr = sb("zr", [2 * KD, HH], F32, first)
        at = sb("at", [2, D], F32, first)
        aT = sb("aT", [2, KD, PAIR], F32R, first)
        xtok = sb("xtok", [2, 2, D], F32, first)
        xb = sb("xb", [2, D], F32, first)
        r = sb("r", [2, D], F32, first)
        stats = sb("stats", [2, 6], F32, first)
        mv = sb("mv", [2, 2], F32, first)
        vare = sb("vare", [2], F32, first)
        rstd = sb("rstd", [2], F32, first)
        rows = sb("rows", [2, 2, TOPK, ROW], F32, first)
        x1T = sb("x1T", [KD, PAIR], F32, first)
        lg = sb("lg", [2, E], F32, first)
        mx = sb("mx", [2, 8], F32, first)
        ix = sb("ix", [2, 8], U32, first)
        ixf = sb("ixf", [2, TOPK], F32, first)
        oh = sb("oh", [2, TOPK, E], F32, first)
        sel = sb("sel", [2, E], BF16, first)
        dl = sb("dl", [2], F32, first)
        el = sb("el", [2], F32, first)
        el1 = sb("el1", [2], F32, first)
        dst = sb("dst", [2, TOPK], F32, first)
        pos8 = sb("pos8", [2, E], F32, first)
        pos16 = sb("pos16", [2, TOPK, E], F32, first)
        posf = sb("posf", [2, TOPK], F32, first)
        idx = sb("idx", [2, 2, TOPK], U32, first)
        first.close()

        late = ExitStack()
        sb("w_place", [EARLY, 2, WE], F32, late)
        w_late_raw = sb("w_late_raw", [LATE, 2, WE], F32, late)
        late.close()
        sb("w_whole_place", [E, 2, WE], F32)
        NXG = 8
        xg = sb("xg", [NXG, ROW])
        xgT = sb("xgT", [2, 2, KD, P], F32R)
        hg = sb("hg", [2, F])
        hT = sb("hT", [2, KF, P], F32R)
        fx = sb("fx", [2, D])
        y = sb("y", [2, D])
        NZ = 4
        NCH = T // (P * NZ)
        z2 = sb("z2", [2, NZ, TOPK, D])
        z = sb("z", [2, NZ, D])
        zo = sb("zo", [2, NZ, D])
        zst = sb("zst", [NZ, 6])
        zmv = sb("zmv", [2, NZ, 2])
        zve = sb("zve", [NZ])
        zrs = sb("zrs", [2, NZ])

        s_const, s_bias, s_proj = sem("s_const"), sem("s_bias"), sem("s_proj")
        s_x = [sem("s_x0"), sem("s_x1")]
        s_tok = [sem("s_tok0"), sem("s_tok1")]
        s_wraw = [sem("s_wraw0"), sem("s_wraw1")]
        s_rows = [sem("s_rows0"), sem("s_rows1")]
        s_tail, s_late = sem("s_tail"), sem("s_late")
        s_xg = [sem(f"s_xg{n}") for n in range(NXG)]
        s_y = [sem("s_y0"), sem("s_y1")]
        s_z = [sem("s_z0"), sem("s_z1")]
        s_out = [sem("s_out0"), sem("s_out1")]
        kv_done, st_done, n_done, t_done = sem("kv_done"), sem("st_done"), sem("n_done"), sem("t_done")
        q_done, w_done, t2_done, l_done = sem("q_done"), sem("w_done"), sem("t2_done"), sem("l_done")
        rank_done, cnt_done, tbl_done = sem("rank_done"), sem("cnt_done"), sem("tbl_done")
        tx_done, h_done, th_done, y_done = sem("tx_done"), sem("h_done"), sem("th_done"), sem("y_done")
        proj_high, xhi_ready, k_ready, tcos_ready = sem("proj_high"), sem("xhi_ready"), sem("k_ready"), sem("tcos_ready")
        x1T_ready, rowcopy_ready, thi_ready = sem("x1T_ready"), sem("rowcopy_ready"), sem("thi_ready")
        e_ready, q32_ready, late_high = sem("e_ready"), sem("q32_ready"), sem("late_high")
        xghi_ready, gelu_ready, hhi_ready = sem("xghi_ready"), sem("gelu_ready"), sem("hhi_ready")
        qhi_ready = sem("qhi_ready")
        dve_const, proj_low, kvb_ready, o_done = sem("dve_const"), sem("proj_low"), sem("kvb_ready"), sem("o_done")
        comb_step, at_ready, tlo_ready, qlo_ready = sem("comb_step"), sem("at_ready"), sem("tlo_ready"), sem("qlo_ready")
        state_step, norm_step, x1_ready = sem("state_step"), sem("norm_step"), sem("x1_ready")
        route_step, pos_step, late_low = sem("route_step"), sem("pos_step"), sem("late_low")
        table_step, xglo_ready, hlo_ready, y_ready = sem("table_step"), sem("xglo_ready"), sem("hlo_ready"), sem("y_ready")
        z_step, zo_ready = sem("z_step"), sem("zo_ready")
        pool_const, xlo_ready, xb_ready = sem("pool_const"), sem("xlo_ready"), sem("xb_ready")
        wprep, pow_step, fx_ready, zpow_step = sem("wprep"), sem("pow_step"), sem("fx_ready"), sem("zpow_step")
        POOL_CONST = 12

        STATE, STATE_READ = 6, 4
        NORM, NORM_R, NORM_MV = 3, 1, 3
        ROUTE, ROUTE_LG, ROUTE_SEL, ROUTE_DL, ROUTE_META = 14, 1, 6, 7, 14
        POS, POS_READ = 4, 1
        TAILS, TABLE_MADE, TABLE = 3, 16, 17
        ZCH, Z_SUM, Z_MV = 3, 1, 3

        block = ctx.enter_context(nc.Block())

        def pipeline(eng, step):
            def loop(first_i, last_i):
                with eng.Fori(first_i // 2, last_i // 2 + 1) as u:
                    step(u, first_i)
                    step(u, first_i + 1)

            def once(i):
                step(i // 2, i)

            once(0)
            once(1)
            loop(2, PB - 1)
            for b in range(1, B):
                once(b * PB)
                once(b * PB + 1)
                if b == 1:
                    once(b * PB + 2)
                    once(b * PB + 3)
                loop(b * PB + (4 if b == 1 else 2), b * PB + PB - (1 if b < B - 1 else 3))
            once(NPAIR - 2)
            once(NPAIR - 1)
            once(NPAIR)
            once(NPAIR + 1)
            loop(NPAIR + 2, NPAIR + PB - 1)
            once(NPAIR + PB)
            once(NPAIR + PB + 1)

        def hold(eng):
            eng.nop(nofuse=True)

        def parts(rep):
            return (rep < NPAIR, LAG <= rep < LAG + NPAIR, LAG < rep <= LAG + NPAIR,
                    rep % PB == 0 and PB <= rep <= NPAIR, PB <= rep < PB + NPAIR)

        def lagged(u, rep):
            slot = (rep - LAG) % 2
            return u * 2 + (rep % 2 - LAG), u + (rep % 2 - LAG - slot) // 2

        def lagged_half(u, rep):
            return u + (rep % 2 - LAG - 1 - (rep - LAG - 1) % 2) // 2

        def weight_expert(u, rep):
            if 2 <= rep < PB:
                return u - 1
            return {PB: 3, 2 * PB: 4, 3 * PB: 5}.get(rep - rep % 2)

        PASSES = ((0, 0), (0, 1), (1, 0))

        @block.sync
        def _(sp):
            sp.dma_start(xraw[:, 0], xT[0].rearrange("p (k t) -> p k t", k=KD)).then_inc(s_x[0], 16)
            for raw, wt in ((rwk, WkT), (rwv, WvT), (rwq, WqT), (rwo, WoT)):
                sp.dma_start(raw[:], wt.rearrange("(k p) f -> p k f", p=P)).then_inc(s_proj, 16)
            sp.dma_start(cst[:], consts).then_inc(s_const, 16)
            sp.dma_start(bkv[:, 0:KD].rearrange("p a b -> p (a b)"), bk.partition_broadcast(P)).then_inc(s_bias, 16)
            sp.dma_start(bkv[:, KD:].rearrange("p a b -> p (a b)"), bv.partition_broadcast(P)).then_inc(s_bias, 16)
            sp.dma_start(bqc[:], bq).then_inc(s_bias, 16)
            sp.dma_start(bob[:], bo.partition_broadcast(P)).then_inc(s_bias, 16)
            sp.dma_start(rw[:], rwT.rearrange("(k p) e -> p k e", p=P)).then_inc(s_bias, 16)

            x_pairs = xT.rearrange("i p (k t) -> i p k t", k=KD)
            tok_pairs = x.rearrange("b l d -> (b l) d").rearrange("(i h p) d -> i p h d", h=2, p=P)
            w_experts = (w1T, w2T)
            for kind in range(2):
                sp.dma_start(wraw[:, kind], w_experts[kind][0]).then_inc(s_wraw[kind], 16)

            def step(u, rep):
                proj, attn, _, _, _ = parts(rep)
                par = rep % 2
                i = u * 2 + par
                if rep < NPAIR - 1:
                    if rep >= 1:
                        sp.wait_ge(xlo_ready, i)
                    sp.dma_start(xraw[:, 1 - par], x_pairs[i + 1]).then_inc(s_x[1 - par], 16)
                if attn:
                    j, _ = lagged(u, rep)
                    slot = (rep - LAG) % 2
                    if rep > LAG + 1:
                        sp.wait_ge(xb_ready, j - 1)
                    sp.dma_start(xtok[:, slot], tok_pairs[j]).then_inc(s_tok[slot], 16)
                e = weight_expert(u, rep)
                if e is not None and rep < 3 * PB:
                    sp.wait_ge(wprep, e * 4 + (2 * par + 2))
                    sp.dma_start(wraw[:, par], w_experts[par][e + 1]).then_inc(s_wraw[par], 16)

            pipeline(sp, step)

            sp.wait_ge(table_step, 1)
            sp.wait_ge(s_rows[0], 16 * 2 * TOPK * (NPAIR // 2))
            sp.wait_ge(s_rows[1], 16 * 2 * TOPK * (NPAIR // 2))
            for n in range(LATE):
                for kind in range(2):
                    sp.dma_start(w_late_raw[:, n, 1, kind * HALF:(kind + 1) * HALF],
                                 w_experts[kind][EARLY + n]).then_inc(s_late, 16)
            sp.wait_ge(table_step, TABLE)
            sp.wait_ge(s_tail, 16 * (E + 1))

            def gather(s, slot):
                row = nc.values_load(steps[1:2, bass.ds(s, 1)], engines=[ENG.SP], min_val=0, max_val=E * REGION)
                sp.dma_start(xg[:, slot], ex[bass.ds(row, P), :]).then_inc(s_xg[slot], 16)

            for s in range(NXG):
                gather(s, s)
            with sp.Fori(1, STEPS // NXG) as u:
                for n in range(NXG):
                    sp.wait_ge(s_y[n % 2], (u * (NXG // 2) + (n // 2 + 1 - NXG // 2)) * 16)
                    gather(u * NXG + n, n)
            sp.wait_ge(s_y[0], 16 * (STEPS // 2))
            sp.wait_ge(s_y[1], 16 * (STEPS // 2))
            y_chunks = yd.rearrange("(c p q k) d -> c p q k d", p=P, q=NZ, k=TOPK)

            def load(c, slot):
                sp.dma_start(z2[:, slot], y_chunks[c]).then_inc(s_z[slot], 16)

            load(0, 0)
            load(1, 1)
            with sp.Fori(0, NCH // 2 - 1) as u:
                for n in range(2):
                    sp.wait_ge(z_step, (u * 2 + n) * ZCH + Z_SUM)
                    load(u * 2 + (n + 2), n)

        @block.tensor
        def _(pe):
            pe.wait_ge(proj_low, 4)
            pe.wait_ge(s_bias, 16 * 5)
            pe.wait_ge(dve_const, 2)
            pe.wait_ge(pool_const, POOL_CONST)
            ident = const("ident")

            def keys_values(i, rep, h):
                t = i * 2 + h
                if h == 0:
                    pe.wait_ge(xlo_ready, i + 1)
                if rep > 0 or h > 0:
                    pe.wait_ge(kvb_ready, t)
                n = 0
                for k in range(KD):
                    for a, b in PASSES:
                        mm = nc.tensor.matmul(PS[:, bKV, :], xs[:, rep % 2, a, k, h * P:(h + 1) * P], wkv[:, b, k, :],
                                              start=(n == 0), stop=(n == 3 * KD - 1))
                        n += 1
                mm.then_inc(kv_done, 1)

            def state(t, rep_t):
                pe.wait_ge(k_ready, t + 1)
                if rep_t % NT_B == 0 and rep_t > 0:
                    pe.wait_ge(state_step, STATE * (rep_t // NT_B - 1) + STATE_READ)
                for half in range(KD):
                    mm = nc.tensor.matmul(PS[:, bST + half, 0:2 * VW], kr[:, rep_t % 2, half, :],
                                          vs[:, rep_t % 2, half].rearrange("p a b -> p (a b)"),
                                          start=(rep_t % NT_B == 0), stop=(rep_t % NT_B == NT_B - 1),
                                          skip_group_check=True)
                mm.then_inc(st_done, 1)

            def attend(j, rep, h):
                if h == 0:
                    pe.wait_ge(qlo_ready, j + 1)
                    if (rep - LAG) % PB == 0:
                        pe.wait_ge(state_step, STATE * ((rep - LAG) // PB + 1))
                if rep > LAG or h > 0:
                    pe.wait_ge(o_done, j * 2 + h)
                for half in range(KD):
                    for n, (a, b) in enumerate(PASSES):
                        mm = nc.tensor.matmul(PS[:, bN + half, 0:2 * NW], qs[:, a, half, h * P:(h + 1) * P],
                                              sts[:, b, half].rearrange("p a b -> p (a b)"),
                                              start=(n == 0), stop=(n == 2))
                mm.then_inc(n_done, 1)

            def x1_transposed(jj, rep):
                pe.wait_ge(x1_ready, jj + 1)
                for h in range(2):
                    for k in range(KD):
                        mm = nc.tensor.transpose(PS[:, bA, k * PAIR + h * P:k * PAIR + (h + 1) * P],
                                                 rows[:, (rep - LAG - 1) % 2, h, 0, k * P:(k + 1) * P], ident)
                mm.then_inc(t2_done, 1)

            def logits(jj):
                pe.wait_ge(x1T_ready, jj + 1)
                for h in range(2):
                    for k in range(KD):
                        mm = nc.tensor.matmul(PS[:, bC, h * E:(h + 1) * E], x1T[:, k, h * P:(h + 1) * P], rw[:, k, :],
                                              start=(k == 0), stop=(k == KD - 1))
                mm.then_inc(l_done, 1)

            def attention_transposed(j):
                pe.wait_ge(at_ready, j + 1)
                for h in range(2):
                    for k in range(KD):
                        mm = nc.tensor.transpose(PS[:, bA, k * PAIR + h * P:k * PAIR + (h + 1) * P],
                                                 at[:, h, k * P:(k + 1) * P], ident)
                mm.then_inc(t_done, 1)

            def queries(i, rep):
                if rep > 0:
                    pe.wait_ge(q32_ready, i)
                for half in range(KD):
                    n = 0
                    for k in range(KD):
                        for a, b in PASSES:
                            mm = nc.tensor.matmul(PS[:, bQ, half * PAIR:(half + 1) * PAIR],
                                                  wq[:, a, k, half * P:(half + 1) * P], xs[:, rep % 2, b, k, :],
                                                  start=(n == 0), stop=(n == 3 * KD - 1))
                            n += 1
                mm.then_inc(q_done, 1)

            def project_out(j, rep):
                pe.wait_ge(tlo_ready, j + 1)
                if rep > LAG:
                    pe.wait_ge(route_step, j * ROUTE + (ROUTE_LG - ROUTE))
                for h in range(2):
                    n = 0
                    for k in range(KD):
                        for a, b in PASSES:
                            mm = nc.tensor.matmul(PS[:, bC, h * D:(h + 1) * D], aT[:, a, k, h * P:(h + 1) * P],
                                                  wo[:, b, k, :], start=(n == 0), stop=(n == 3 * KD - 1))
                            n += 1
                mm.then_inc(w_done, 1)

            def rank(jj, rep):
                pe.wait_ge(route_step, jj * ROUTE + ROUTE_SEL)
                before = cum[:, (rep - LAG - 1) % 2, :]
                for h in range(2):
                    out_h = PS[:, bA, h * E:(h + 1) * E]
                    nc.tensor.matmul(out_h, ones_bf[:], before, start=True, stop=False)
                    if h == 1:
                        nc.tensor.matmul(out_h, ones_bf[:], sel[:, 0, :], start=False, stop=False)
                    mm = nc.tensor.matmul(out_h, before_bf[:], sel[:, h, :], start=False, stop=True)
                mm.then_inc(rank_done, 1)

            def step(u, rep):
                proj, attn, route, _, _ = parts(rep)
                i = u * 2 + rep % 2
                j = lagged(u, rep)[0]
                if proj:
                    keys_values(i, rep, 0)
                if attn:
                    attend(j, rep, 0)
                if 1 <= rep <= NPAIR:
                    state(i * 2 - 1, 2 * rep - 1)
                if attn:
                    attend(j, rep, 1)
                if route:
                    x1_transposed(j - 1, rep)
                if proj:
                    keys_values(i, rep, 1)
                if route:
                    logits(j - 1)
                if proj:
                    state(i * 2, 2 * rep)
                if attn:
                    attention_transposed(j)
                if proj:
                    queries(i, rep)
                if attn:
                    project_out(j, rep)
                if route:
                    rank(j - 1, rep)

            pipeline(pe, step)

            pe.wait_ge(pos_step, NPAIR * POS)
            pe.wait_ge(route_step, NPAIR * ROUTE)
            nc.tensor.matmul(PS[:, bA, 0:E], ones_bf[:], cum[:, 0, :], start=True, stop=True).then_inc(cnt_done, 1)
            pe.wait_ge(table_step, TABLE_MADE)
            for c in range(2):
                mm = nc.tensor.matmul(PS[0:2, bQ, c * P:(c + 1) * P], table[:, c, :], ident, start=True, stop=True)
            mm.then_inc(tbl_done, 1)

            def rows_transposed(s, s4, n):
                pe.wait_ge(s_xg[n], s4 * 16 + 16)
                if not (isinstance(s, int) and s < 2):
                    pe.wait_ge(xglo_ready, s - 1)
                for k in range(KD):
                    mm = nc.tensor.transpose(PS[:, gX + n % 2, k * P:(k + 1) * P], xg[:, n, k * P:(k + 1) * P], ident)
                mm.then_inc(tx_done, 1)

            def hidden(s, n, e):
                pe.wait_ge(xglo_ready, s + 1)
                if not (isinstance(s, int) and s < 2):
                    pe.wait_ge(gelu_ready, s - 1)
                m = 0
                for k in range(KD):
                    for a, b in PASSES:
                        mm = nc.tensor.matmul(PS[:, gH + n % 2, :], xgT[:, n % 2, a, k, :],
                                              w[:, bass.ds(e, 1), b, k * F:(k + 1) * F].rearrange("p o f -> p (o f)"),
                                              start=(m == 0), stop=(m == 3 * KD - 1))
                        m += 1
                mm.then_inc(h_done, 1)

            def outputs(s, n, e):
                pe.wait_ge(hlo_ready, s + 1)
                if not (isinstance(s, int) and s < 2):
                    pe.wait_ge(y_ready, s - 1)
                m = 0
                for k in range(KF):
                    for a, b in PASSES:
                        mm = nc.tensor.matmul(PS[:, gY + n % 2, 0:D], hT[:, a, k, :],
                                              w[:, bass.ds(e, 1), b, HALF + k * D:HALF + (k + 1) * D]
                                              .rearrange("p o f -> p (o f)"),
                                              start=(m == 0), stop=(m == 3 * KF - 1))
                        m += 1
                mm.then_inc(y_done, 1)

            def hidden_transposed(s, n):
                pe.wait_ge(gelu_ready, s + 1)
                if not (isinstance(s, int) and s < 2):
                    pe.wait_ge(hlo_ready, s - 1)
                for k in range(KF):
                    mm = nc.tensor.transpose(PS[:, gT + n % 2, k * P:(k + 1) * P], hg[:, n % 2, k * P:(k + 1) * P], ident)
                mm.then_inc(th_done, 1)

            def expert(s):
                return nc.values_load(steps[0:1, bass.ds(s, 1)], engines=[ENG.PE], min_val=0, max_val=E - 1)

            def ffn(u, first_group, last_group):
                for n in range(NXG):
                    s = u * NXG + n
                    if not (last_group and n == NXG - 1):
                        rows_transposed(s + 1, u + (n + 1) // NXG, (n + 1) % NXG)
                    hidden(s, n, expert(s))
                    if not (first_group and n == 0):
                        outputs(s - 1, (n - 1) % NXG, expert(s - 1))
                    hidden_transposed(s, n)

            pe.wait_ge(table_step, TABLE)
            pe.wait_ge(late_low, 2 * LATE)
            rows_transposed(0, 0, 0)
            ffn(0, True, False)
            with pe.Fori(1, STEPS // NXG - 1) as u:
                ffn(u, False, False)
            ffn(STEPS // NXG - 1, False, True)
            outputs(STEPS - 1, NXG - 1, expert(STEPS - 1))

        @block.scalar
        def _(act):
            act.wait_ge(s_proj, 16 * 4)
            for n, (dst_w, raw) in enumerate(((wkv[:, 0, :, 0:D], rwk), (wkv[:, 0, :, D:], rwv), (wq[:, 0], rwq), (wo[:, 0], rwo))):
                nc.scalar.activation(dst_w, raw[:], ACT.Copy).then_inc(proj_high, 1)
            act.wait_ge(pool_const, POOL_CONST)
            act.dma_start(ex[E * REGION:, :], tail[:]).then_inc(s_tail, 16)
            act.wait_ge(s_const, 16)
            act.wait_ge(s_bias, 16 * 5)

            def x_high(i, rep, count):
                act.wait_ge(s_x[rep % 2], count)
                if rep >= 2:
                    act.wait_ge(q_done, i - 1)
                nc.scalar.activation(xs[:, rep % 2, 0], xraw[:, rep % 2], ACT.Copy).then_inc(xhi_ready, 1)

            def cos_part(j, rep, h):
                act.wait_ge(n_done, j * 2 + (h + 1))
                if rep > LAG or h > 0:
                    act.wait_ge(o_done, j * 2 + h)
                t = (2 * (rep - LAG) + h) % NT_B
                col = (j * 2 + h) - (2 * (rep - LAG) + h - t)
                nc.scalar.activation(tcos[:], PS[:, bN:bN + KD, NW:2 * NW], ACT.Copy,
                                     scale=cos_col(col)).then_inc(tcos_ready, 1)

            def cos_col(t):
                return cst[:, bass.ds(t + CO["cos"][0], 1)]

            def sin_col(t):
                return cst[:, bass.ds(t + CO["sin"][0], 1)]

            def keys_scaled_values(i, rep, h):
                t = i * 2 + h
                act.wait_ge(kvb_ready, t + 1)
                if rep > 0:
                    act.wait_ge(st_done, t - 1)
                in_batch = t - (2 * rep + h - (2 * rep + h) % NT_B)
                nc.scalar.activation(kr[:, h], kvb[:, h, 0:KD, 0:P], ACT.Relu)
                nc.scalar.activation(vs[:, h, :, 0, :], kvb[:, h, KD:, :], ACT.Copy, scale=sin_col(in_batch))
                nc.scalar.activation(vs[:, h, :, 1, :], kvb[:, h, KD:, :], ACT.Copy, scale=cos_col(in_batch))\
                    .then_inc(k_ready, 1)

            def step(u, rep):
                proj, attn, route, _, qsplit = parts(rep)
                par = rep % 2
                i = u * 2 + par
                j = lagged(u, rep)[0]
                if attn:
                    cos_part(j, rep, 0)
                if proj:
                    keys_scaled_values(i, rep, 0)
                if attn:
                    cos_part(j, rep, 1)
                if route:
                    act.wait_ge(t2_done, j)
                    if rep > LAG + 1:
                        act.wait_ge(l_done, j - 1)
                    nc.scalar.activation(x1T[:].rearrange("p k t -> p (k t)"), PS[:, bA, :], ACT.Copy).then_inc(x1T_ready, 1)
                    slot = (rep - LAG - 1) % 2
                    nc.scalar.activation(rows[:, slot, :, 1, 0:D], rows[:, slot, :, 0, 0:D], ACT.Copy).then_inc(rowcopy_ready, 1)
                if rep < NPAIR - 1:
                    x_high(i + 1, rep + 1, u * 16 + (16 if par == 0 else 32))
                if proj:
                    keys_scaled_values(i, rep, 1)
                if attn:
                    act.wait_ge(t_done, j + 1)
                    if rep > LAG:
                        act.wait_ge(w_done, j)
                    nc.scalar.activation(aT[:, 0].rearrange("p k t -> p (k t)"), PS[:, bA, :], ACT.Copy).then_inc(thi_ready, 1)
                if qsplit:
                    act.wait_ge(q32_ready, i - (PB - 1))
                    if attn:
                        act.wait_ge(n_done, j * 2 + 2)
                    hold(act)
                    place = i - rep // PB * PB
                    nc.scalar.activation(qs[:, 0], q32[:, bass.ds(place, 1)].rearrange("p o k t -> p (o k) t"), ACT.Copy)\
                        .then_inc(qhi_ready, 1)
                if route:
                    act.wait_ge(route_step, (j - 1) * ROUTE + ROUTE_DL)
                    nc.scalar.activation(el[:], dl[:], ACT.Exp).then_inc(e_ready, 1)
                if proj:
                    act.wait_ge(q_done, i + 1)
                    if rep >= PB:
                        act.wait_ge(qlo_ready, i - (PB - 1))
                    hold(act)
                    place = i - rep // PB * PB
                    for half in range(KD):
                        a = nc.scalar.activation(q32[:, bass.ds(place, 1), half, :].rearrange("p o t -> p (o t)"),
                                                 PS[:, bQ, half * PAIR:(half + 1) * PAIR],
                                                 ACT.Relu, bias=bqc[:, half:half + 1])
                    a.then_inc(q32_ready, 1)

            x_high(0, 0, 16)
            pipeline(act, step)

            act.wait_ge(table_step, TAILS)
            for e in range(E):
                row = nc.values_load(tails_i[0:1, e:e + 1], engines=[ENG.Activation], min_val=0, max_val=E * REGION - P)
                act.dma_start(ex[bass.ds(row, P), :], tail[:]).then_inc(s_tail, 16)
            act.wait_ge(s_late, 16 * 2 * LATE)
            for n in range(LATE):
                nc.scalar.activation(w[:, EARLY + n, 0, :], w_late_raw[:, n, 1, :], ACT.Copy).then_inc(late_high, 1)

            def rows_high(s, n):
                act.wait_ge(tx_done, s + 1)
                nc.scalar.activation(xgT[:, n % 2, 0].rearrange("p k t -> p (k t)"), PS[:, gX + n % 2, 0:D], ACT.Copy)\
                    .then_inc(xghi_ready, 1)

            def ffn(u, last_group):
                for n in range(NXG):
                    s = u * NXG + n
                    act.wait_ge(h_done, s + 1)
                    nc.scalar.activation(hg[:, n % 2, :], PS[:, gH + n % 2, :], ACT.Gelu).then_inc(gelu_ready, 1)
                    if not (last_group and n == NXG - 1):
                        rows_high(s + 1, n + 1)
                    act.wait_ge(th_done, s + 1)
                    nc.scalar.activation(hT[:, 0].rearrange("p k t -> p (k t)"), PS[:, gT + n % 2, :], ACT.Copy)\
                        .then_inc(hhi_ready, 1)

            rows_high(0, 0)
            with act.Fori(0, STEPS // NXG - 1) as u:
                ffn(u, False)
            ffn(STEPS // NXG - 1, True)

            o_chunks = out.rearrange("b l d -> (b l) d").rearrange("(c p q) d -> c p q d", p=P, q=NZ)
            with act.Fori(0, NCH // 2) as u:
                for n in range(2):
                    act.wait_ge(zo_ready, u * 2 + (n + 1))
                    act.dma_start(o_chunks[u * 2 + n], zo[:, n]).then_inc(s_out[n], 16)
            act.wait_ge(s_out[0], 16 * NCH // 2)
            act.wait_ge(s_out[1], 16 * NCH // 2)

        @block.vector
        def _(dve):
            dve.wait_ge(s_proj, 16 * 4)
            for n, (hi, lo, raw) in enumerate(((wkv[:, 0, :, 0:D], wkv[:, 1, :, 0:D], rwk),
                                               (wkv[:, 0, :, D:], wkv[:, 1, :, D:], rwv),
                                               (wq[:, 0], wq[:, 1], rwq), (wo[:, 0], wo[:, 1], rwo))):
                dve.wait_ge(proj_high, n + 1)
                nc.vector.tensor_tensor(lo, raw[:], hi.bitcast(F32), ALU.subtract).then_inc(proj_low, 1)
            dve.wait_ge(s_const, 16)
            nc.vector.tensor_copy(before_bf[:], const("before")).then_inc(dve_const, 1)
            nc.vector.tensor_scalar(dst[:].rearrange("p a b -> p (a b)"), const("dst"), float(-TOPK * PAIR), None, ALU.add)\
                .then_inc(dve_const, 1)
            dve.wait_ge(dve_const, 2)
            dve.wait_ge(s_bias, 16 * 5)
            dve.wait_ge(pool_const, POOL_CONST)

            def add_bias(i, rep, h):
                t = i * 2 + h
                dve.wait_ge(kv_done, t + 1)
                if rep > 0:
                    dve.wait_ge(k_ready, t - 1)
                nc.vector.tensor_tensor(kvb[:, h, :, 0:P], PS[:, bKV, :].rearrange("p (a b) -> p a b", b=P), bkv[:],
                                        ALU.add).then_inc(kvb_ready, 1)

            def add_sin_part(j, rep, h):
                dve.wait_ge(tcos_ready, j * 2 + (h + 1))
                t = (2 * (rep - LAG) + h) % NT_B
                col = (j * 2 + h) - (2 * (rep - LAG) + h - t)
                nc.vector.scalar_tensor_tensor(out=o[:, h], in0=PS[:, bN:bN + KD, 0:NW],
                                               scalar=cst[:, bass.ds(col + CO["sin"][0], 1)], in1=tcos[:],
                                               op0=ALU.mult, op1=ALU.add).then_inc(o_done, 1)

            def normalise_attention(j, rep):
                ov = o[:].rearrange("p h k n -> p (h k) n")
                dve.wait_ge(o_done, j * 2 + 2)
                nc.vector.tensor_scalar(den[:], ov[:, :, P:NW], ATT_EPS, None, ALU.max).then_inc(comb_step, 1)
                dve.wait_ge(comb_step, j * 2 + 1)
                nc.vector.reciprocal(zr[:], den[:]).then_inc(comb_step, 1)
                dve.wait_ge(comb_step, j * 2 + 2)
                if rep > LAG:
                    dve.wait_ge(t_done, j)
                nc.vector.tensor_tensor(at[:].rearrange("p h (k a b) -> p (h k) a b", a=HH, b=HD),
                                        ov[:, :, 0:P].rearrange("p m (a b) -> p m a b", b=HD),
                                        zr[:].unsqueeze(3).broadcast_to([P, 2 * KD, HH, HD]), ALU.mult)\
                    .then_inc(at_ready, 1)

            def split_state(b, i, rep, attn, j):
                dve.wait_ge(st_done, i * 2)
                for half in range(KD):
                    ps = PS[:, bST + half, 0:2 * VW].rearrange("p (a b) -> p a b", b=VW)
                    nc.vector.tensor_tensor(st32[:, half, :, 0:P], ps[:, :, 0:P],
                                            const("block").unsqueeze(1).broadcast_to([P, 2, P]), ALU.mult)\
                        .then_inc(state_step, 1)
                    nc.vector.tensor_tensor(st32[:, half, :, P:NW], ps[:, :, P:VW].broadcast_to([P, 2, HH]),
                                            const("heads").unsqueeze(1).broadcast_to([P, 2, HH]), ALU.mult)\
                        .then_inc(state_step, 1)
                dve.wait_ge(state_step, STATE * b + 4)
                if attn:
                    dve.wait_ge(n_done, j * 2 + 2)
                nc.vector.tensor_copy(sts[:, 0], st32[:]).then_inc(state_step, 1)
                dve.wait_ge(state_step, STATE * b + 5)
                nc.vector.tensor_tensor(sts[:, 1], st32[:], sts[:, 0].bitcast(F32), ALU.subtract).then_inc(state_step, 1)

            def choose(jj, rep):
                base = jj * ROUTE
                dve.wait_ge(l_done, jj + 1)
                nc.vector.tensor_copy(lg[:].rearrange("p a b -> p (a b)"), PS[:, bC, 0:2 * E]).then_inc(route_step, 1)
                dve.wait_ge(route_step, base + 1)
                hold(dve)
                nc.vector.max(mx[:, 0, :], lg[:, 0, :])
                nc.vector.max(mx[:, 1, :], lg[:, 1, :]).then_inc(route_step, 1)
                dve.wait_ge(route_step, base + 2)
                hold(dve)
                nc.vector.max_index(ix[:, 0, :], mx[:, 0, :], lg[:, 0, :])
                nc.vector.max_index(ix[:, 1, :], mx[:, 1, :], lg[:, 1, :]).then_inc(route_step, 1)
                dve.wait_ge(route_step, base + 3)
                nc.vector.tensor_copy(ixf[:], ix[:, :, 0:TOPK]).then_inc(route_step, 1)
                dve.wait_ge(route_step, base + 4)
                nc.vector.tensor_tensor(oh[:].rearrange("p h k e -> p (h k) e"),
                                        const("experts").unsqueeze(1).broadcast_to([P, 2 * TOPK, E]),
                                        ixf[:].rearrange("p h k -> p (h k)").unsqueeze(2).broadcast_to([P, 2 * TOPK, E]),
                                        ALU.is_equal).then_inc(route_step, 1)
                dve.wait_ge(route_step, base + 5)
                nc.vector.tensor_tensor(sel[:], oh[:, :, 0, :], oh[:, :, 1, :], ALU.add).then_inc(route_step, 1)
                nc.vector.tensor_tensor(dl[:], mx[:, :, 1], mx[:, :, 0], ALU.subtract).then_inc(route_step, 1)

            def gates(jj, rep, slot):
                base = jj * ROUTE
                c0, c1 = cum[:, slot, :], cum[:, 1 - slot, :]
                dve.wait_ge(route_step, base + 7)
                nc.vector.tensor_tensor(c1, c0, sel[:, 0, :], ALU.add).then_inc(route_step, 1)
                dve.wait_ge(route_step, base + 8)
                nc.vector.tensor_tensor(c1, c1, sel[:, 1, :], ALU.add).then_inc(route_step, 1)
                dve.wait_ge(e_ready, jj + 1)
                nc.vector.tensor_scalar(el1[:], el[:], 1.0, None, ALU.add).then_inc(route_step, 1)
                dve.wait_ge(route_step, base + 10)
                nc.vector.reciprocal(rows[:, slot, :, 0, C_GATE], el1[:]).then_inc(route_step, 1)
                dve.wait_ge(route_step, base + 11)
                nc.vector.tensor_tensor(rows[:, slot, :, 1, C_GATE], rows[:, slot, :, 0, C_GATE], el[:], ALU.mult)\
                    .then_inc(route_step, 1)
                nc.vector.tensor_scalar(dst[:], dst[:], float(TOPK * PAIR), None, ALU.add).then_inc(route_step, 1)
                dve.wait_ge(route_step, base + 13)
                nc.vector.tensor_copy(rows[:, slot, :, :, C_DST].bitcast(U32), dst[:]).then_inc(route_step, 1)

            def residual_stats(j, rep):
                dve.wait_ge(w_done, j + 1)
                dve.wait_ge(xb_ready, j + 1)
                nc.vector.tensor_tensor(r[:].rearrange("p h d -> p (h d)"), PS[:, bC, :],
                                        xb[:].rearrange("p h d -> p (h d)"), ALU.add).then_inc(norm_step, 1)
                dve.wait_ge(norm_step, j * NORM + 1)
                nc.vector.bn_stats(stats[:, 0, :], r[:, 0, :])
                nc.vector.bn_stats(stats[:, 1, :], r[:, 1, :]).then_inc(norm_step, 1)
                dve.wait_ge(norm_step, j * NORM + 2)
                hold(dve)
                nc.vector.bn_aggr(mv[:, 0, :], stats[:, 0, :])
                nc.vector.bn_aggr(mv[:, 1, :], stats[:, 1, :]).then_inc(norm_step, 1)

            def positions(jj, slot):
                base = jj * POS
                dve.wait_ge(rank_done, jj + 1)
                nc.vector.tensor_tensor(pos8[:], PS[:, bA, 0:2 * E].rearrange("p (a b) -> p a b", b=E),
                                        const("region").unsqueeze(1).broadcast_to([P, 2, E]), ALU.add).then_inc(pos_step, 1)
                dve.wait_ge(pos_step, base + 1)
                nc.vector.tensor_tensor(pos16[:], oh[:], pos8[:].unsqueeze(2).broadcast_to([P, 2, TOPK, E]), ALU.mult)\
                    .then_inc(pos_step, 1)
                dve.wait_ge(pos_step, base + 2)
                nc.vector.tensor_reduce(posf[:], pos16[:], AX_X, ALU.add).then_inc(pos_step, 1)
                dve.wait_ge(pos_step, base + 3)
                nc.vector.tensor_copy(idx[:, slot], posf[:]).then_inc(pos_step, 1)

            def normalise(j, j2, rep, slot):
                dve.wait_ge(pow_step, j * 2 + 2)
                if rep > LAG + 1:
                    dve.wait_ge(s_rows[slot], j2 * (16 * 2 * TOPK))
                for h in range(2):
                    a = nc.vector.tensor_scalar(rows[:, slot, h, 0, 0:D], r[:, h, :], mv[:, h, 0:1], rstd[:, h:h + 1],
                                                ALU.subtract, ALU.mult)
                a.then_inc(x1_ready, 1)

            def step(u, rep):
                proj, attn, route, whole, qsplit = parts(rep)
                par = rep % 2
                i = u * 2 + par
                j, j2 = lagged(u, rep)
                slot = (rep - LAG) % 2
                if proj:
                    add_bias(i, rep, 0)
                if attn:
                    add_sin_part(j, rep, 0)
                if route:
                    normalise(j - 1, lagged_half(u, rep), rep - 1, 1 - slot)
                if attn:
                    add_sin_part(j, rep, 1)
                    normalise_attention(j, rep)
                if whole:
                    split_state(rep // PB - 1, i, rep, attn, j)
                if proj:
                    add_bias(i, rep, 1)
                if route:
                    choose(j - 1, rep)
                if attn:
                    dve.wait_ge(thi_ready, j + 1)
                    nc.vector.tensor_tensor(aT[:, 1].rearrange("p k t -> p (k t)"), PS[:, bA, :],
                                            aT[:, 0].rearrange("p k t -> p (k t)").bitcast(F32), ALU.subtract)\
                        .then_inc(tlo_ready, 1)
                if route:
                    gates(j - 1, rep, 1 - slot)
                if qsplit:
                    dve.wait_ge(qhi_ready, i - (PB - 1))
                    place = i - rep // PB * PB
                    nc.vector.tensor_tensor(qs[:, 1], q32[:, bass.ds(place, 1)].rearrange("p o k t -> p (o k) t"),
                                            qs[:, 0].bitcast(F32), ALU.subtract).then_inc(qlo_ready, 1)
                if attn:
                    residual_stats(j, rep)
                if route:
                    positions(j - 1, 1 - slot)

            pipeline(dve, step)

            def made(n):
                dve.wait_ge(table_step, n)

            dve.wait_ge(cnt_done, 1)
            nc.vector.tensor_copy(cnt[:], PS[:, bA, 0:E]).then_inc(table_step, 1)
            made(1)
            nc.vector.tensor_tensor(tails_f[:], cnt[:], const("region"), ALU.add).then_inc(table_step, 1)
            made(2)
            nc.vector.tensor_copy(tails_i[:], tails_f[:]).then_inc(table_step, 1)
            nc.vector.tensor_scalar(cnt_i[:], cnt[:], float(P - 1), None, ALU.add).then_inc(table_step, 1)
            made(4)
            nc.vector.tensor_scalar(tiles_i[:], cnt_i[:], P.bit_length() - 1, None, ALU.arith_shift_right).then_inc(table_step, 1)
            made(5)
            nc.vector.tensor_copy(tiles_f[:], tiles_i[:]).then_inc(table_step, 1)
            made(6)
            nc.vector.tensor_tensor(upto[:], const("upto").rearrange("p (a b) -> p a b", b=E),
                                    tiles_f[:].unsqueeze(1).broadcast_to([P, E, E]), ALU.mult).then_inc(table_step, 1)
            made(7)
            nc.vector.tensor_reduce(ends[:], upto[:], AX_X, ALU.add).then_inc(table_step, 1)
            nc.vector.tensor_scalar(jump[:], tiles_f[:], float(-P), float(REGION), ALU.mult, ALU.add).then_inc(table_step, 1)
            made(9)
            nc.vector.tensor_tensor(past[:], const("step").unsqueeze(2).broadcast_to([P, 2, E]),
                                    ends[:].unsqueeze(1).broadcast_to([P, 2, E]), ALU.is_ge).then_inc(table_step, 1)
            made(10)
            nc.vector.tensor_tensor(past_j[:], past[:], jump[:].unsqueeze(1).broadcast_to([P, 2, E]), ALU.mult)\
                .then_inc(table_step, 1)
            made(11)
            nc.vector.tensor_reduce(sums[:, :, 0], past[:], AX_X, ALU.add).then_inc(table_step, 1)
            nc.vector.tensor_reduce(sums[:, :, 1], past_j[:], AX_X, ALU.add).then_inc(table_step, 1)
            made(13)
            nc.vector.tensor_scalar(table[:, :, 0], sums[:, :, 0], float(E - 1), None, ALU.min).then_inc(table_step, 1)
            nc.vector.scalar_tensor_tensor(out=table[:, :, 1], in0=const("step"), scalar=float(P), in1=sums[:, :, 1],
                                           op0=ALU.mult, op1=ALU.add).then_inc(table_step, 1)
            made(15)
            nc.vector.tensor_scalar(table[:, :, 1], table[:, :, 1], float(E * REGION), None, ALU.min).then_inc(table_step, 1)
            dve.wait_ge(tbl_done, 1)
            nc.vector.tensor_copy(steps[0:2, :], PS[0:2, bQ, 0:2 * P]).then_inc(table_step, 1)
            for n in range(LATE):
                dve.wait_ge(late_high, n + 1)
                nc.vector.tensor_tensor(w[:, EARLY + n, 1, :], w_late_raw[:, n, 1, :], w[:, EARLY + n, 0, :].bitcast(F32),
                                        ALU.subtract).then_inc(late_low, 2)

            def rows_low(s, n):
                dve.wait_ge(xghi_ready, s + 1)
                nc.vector.tensor_tensor(xgT[:, n % 2, 1].rearrange("p k t -> p (k t)"), PS[:, gX + n % 2, 0:D],
                                        xgT[:, n % 2, 0].rearrange("p k t -> p (k t)").bitcast(F32), ALU.subtract)\
                    .then_inc(xglo_ready, 1)

            def gated(s, s2, n, early):
                dve.wait_ge(y_done, s + 1)
                dve.wait_ge(fx_ready, s + 1)
                if not early:
                    dve.wait_ge(s_y[n % 2], s2 * 16)
                nc.vector.scalar_tensor_tensor(out=y[:, n % 2, :], in0=PS[:, gY + n % 2, 0:D],
                                               scalar=xg[:, n % NXG, C_GATE:C_GATE + 1], in1=fx[:, n % 2, :],
                                               op0=ALU.mult, op1=ALU.add).then_inc(y_ready, 1)

            def ffn(u, first_group, last_group):
                for n in range(NXG):
                    s = u * NXG + n
                    if not (last_group and n == NXG - 1):
                        rows_low(s + 1, n + 1)
                    if not (first_group and n == 0):
                        gated(s - 1, u * (NXG // 2) + (n - 1) // 2, n - 1, first_group and n <= 2)
                    dve.wait_ge(hhi_ready, s + 1)
                    nc.vector.tensor_tensor(hT[:, 1].rearrange("p k t -> p (k t)"), PS[:, gT + n % 2, :],
                                            hT[:, 0].rearrange("p k t -> p (k t)").bitcast(F32), ALU.subtract)\
                        .then_inc(hlo_ready, 1)

            rows_low(0, 0)
            ffn(0, True, False)
            with dve.Fori(1, STEPS // NXG - 1) as u:
                ffn(u, False, False)
            ffn(STEPS // NXG - 1, False, True)
            gated(STEPS - 1, (STEPS - 1) // 2, NXG - 1, False)

            def sum_stats(c, c2, n, early):
                dve.wait_ge(s_z[n], c2 * 16 + 16)
                if not early:
                    dve.wait_ge(zo_ready, c - 1)
                nc.vector.tensor_tensor(z[:, n], z2[:, n, :, 0, :], z2[:, n, :, 1, :], ALU.add).then_inc(z_step, 1)
                dve.wait_ge(z_step, c * ZCH + 1)
                for q in range(NZ):
                    a = nc.vector.bn_stats(zst[:, q, :], z[:, n, q, :])
                a.then_inc(z_step, 1)
                dve.wait_ge(z_step, c * ZCH + 2)
                hold(dve)
                for q in range(NZ):
                    a = nc.vector.bn_aggr(zmv[:, n, q, :], zst[:, q, :])
                a.then_inc(z_step, 1)

            def finish(c, c2, n, early):
                dve.wait_ge(zpow_step, c * 2 + 2)
                if not early:
                    dve.wait_ge(s_out[n], c2 * 16)
                for q in range(NZ):
                    a = nc.vector.tensor_scalar(zo[:, n, q, :], z[:, n, q, :], zmv[:, n, q, 0:1], zrs[:, n, q:q + 1],
                                                ALU.subtract, ALU.mult)
                a.then_inc(zo_ready, 1)

            sum_stats(0, 0, 0, True)
            sum_stats(1, 0, 1, True)
            finish(0, 0, 0, True)
            sum_stats(2, 1, 0, False)
            finish(1, 0, 1, True)
            with dve.Fori(1, NCH // 2 - 1) as u:
                sum_stats(u * 2 + 1, u, 1, False)
                finish(u * 2, u, 0, False)
                sum_stats(u * 2 + 2, u + 1, 0, False)
                finish(u * 2 + 1, u, 1, False)
            sum_stats(NCH - 1, NCH // 2 - 1, 1, False)
            finish(NCH - 2, NCH // 2 - 1, 0, False)
            finish(NCH - 1, NCH // 2 - 1, 1, False)

        @block.gpsimd
        def _(pool):
            nc.gpsimd.memset(kvb[:, :, :, P:VW], 1.0).then_inc(pool_const, 1)
            nc.gpsimd.memset(half_neg[:], -0.5).then_inc(pool_const, 1)
            nc.gpsimd.memset(ones_bf[:], 1.0).then_inc(pool_const, 1)
            nc.gpsimd.memset(cum[:], 0.0).then_inc(pool_const, 1)
            nc.gpsimd.memset(tail[:, 0:C_DST], 0.0).then_inc(pool_const, 1)
            nc.gpsimd.memset(tail[:, C_DST:C_GATE].bitcast(U32), NO_ROW).then_inc(pool_const, 1)
            nc.gpsimd.memset(tail[:, C_GATE:], 0.0).then_inc(pool_const, 1)
            nc.gpsimd.memset(rows[:, 0, :, 0, C_FLAG], 1.0).then_inc(pool_const, 1)
            nc.gpsimd.memset(rows[:, 1, :, 0, C_FLAG], 1.0).then_inc(pool_const, 1)
            nc.gpsimd.memset(rows[:, 0, :, 1, C_FLAG], 0.0).then_inc(pool_const, 1)
            nc.gpsimd.memset(rows[:, 1, :, 1, C_FLAG], 0.0).then_inc(pool_const, 1)
            nc.gpsimd.memset(rows[:, :, :, :, C_FLAG + 1].rearrange("p a b c -> p (a b c)"), 0.0).then_inc(pool_const, 1)
            pool.wait_ge(pool_const, POOL_CONST)
            pool.wait_ge(s_bias, 16 * 5)

            def x_low(i, rep):
                pool.wait_ge(xhi_ready, i + 1)
                nc.gpsimd.tensor_tensor(xs[:, rep % 2, 1], xraw[:, rep % 2], xs[:, rep % 2, 0].bitcast(F32), ALU.subtract)\
                    .then_inc(xlo_ready, 1)

            def scatter(jj, slot):
                pool.wait_ge(pos_step, (jj + 1) * POS)
                pool.wait_ge(route_step, (jj + 1) * ROUTE)
                pool.wait_ge(rowcopy_ready, jj + 1)
                hold(pool)
                for h in range(2):
                    for k in range(TOPK):
                        nc.gpsimd.indirect_dma_start(ex, bass.IndirectOffsetOnAxis(ap=idx[:, slot, h, k:k + 1], axis=0),
                                                     rows[:, slot, h, k, :], None).then_inc(s_rows[slot], 16)

            def step(u, rep):
                proj, attn, route, whole, qsplit = parts(rep)
                par = rep % 2
                i = u * 2 + par
                j, j2 = lagged(u, rep)
                slot = (rep - LAG) % 2
                if rep < NPAIR - 1:
                    x_low(i + 1, rep + 1)
                if attn:
                    pool.wait_ge(s_tok[slot], j2 * 16 + 16)
                    if rep > LAG:
                        pool.wait_ge(norm_step, j * NORM + (NORM_R - NORM))
                    nc.gpsimd.tensor_tensor(xb[:], xtok[:, slot], bob[:].unsqueeze(1).broadcast_to([P, 2, D]), ALU.add)\
                        .then_inc(xb_ready, 1)
                e = weight_expert(u, rep)
                if e is not None:
                    pool.wait_ge(s_wraw[par], e * 16 + 16)
                    if rep == 2:
                        pool.wait_ge(proj_low, 4)
                    c0 = par * HALF
                    w_hi, w_lo = (w[:, bass.ds(e, 1), part, c0:c0 + HALF].rearrange("p o f -> p (o f)")
                                  for part in range(2))
                    nc.gpsimd.tensor_copy(w_hi, wraw[:, par]).then_inc(wprep, 1)
                    pool.wait_ge(wprep, e * 4 + (2 * par + 1))
                    nc.gpsimd.tensor_tensor(w_lo, wraw[:, par], w_hi.bitcast(F32), ALU.subtract).then_inc(wprep, 1)
                if attn:
                    pool.wait_ge(norm_step, j * NORM + NORM_MV)
                    hold(pool)
                    nc.gpsimd.tensor_scalar(vare[:], mv[:, :, 1], LN_EPS, None, ALU.add).then_inc(pow_step, 1)
                    pool.wait_ge(pow_step, j * 2 + 1)
                    nc.gpsimd.tensor_tensor(rstd[:], vare[:], half_neg[:, 0:2], ALU.pow).then_inc(pow_step, 1)
                if route:
                    scatter(j - 1, 1 - slot)

            x_low(0, 0)
            pipeline(pool, step)

            def residual(s, s4, n, early):
                pool.wait_ge(s_xg[n % NXG], s4 * 16 + 16)
                if not early:
                    pool.wait_ge(y_ready, s - 1)
                hold(pool)
                nc.gpsimd.tensor_scalar(fx[:, n % 2, :], xg[:, n % NXG, 0:D], xg[:, n % NXG, C_FLAG:C_FLAG + 1], 1.0,
                                        ALU.mult, ALU.mult).then_inc(fx_ready, 1)

            def send(s, n):
                pool.wait_ge(y_ready, s + 1)
                hold(pool)
                nc.gpsimd.indirect_dma_start(yd, bass.IndirectOffsetOnAxis(ap=xg[:, n, C_DST:C_GATE].bitcast(U32), axis=0),
                                             y[:, n % 2, :], None, bounds_check=TOPK * T - 1, oob_is_err=False)\
                    .then_inc(s_y[n % 2], 16)

            def ffn(u, first_group, last_group):
                for n in range(NXG):
                    if not (last_group and n == NXG - 1):
                        residual(u * NXG + (n + 1), u + (n + 1) // NXG, n + 1, first_group and n == 0)
                    send(u * NXG + n, n)

            residual(0, 0, 0, True)
            ffn(0, True, False)
            with pool.Fori(1, STEPS // NXG - 1) as u:
                ffn(u, False, False)
            ffn(STEPS // NXG - 1, False, True)

            def deviation(c, n, early):
                pool.wait_ge(z_step, c * ZCH + Z_MV)
                if not early:
                    pool.wait_ge(zpow_step, c * 2)
                hold(pool)
                nc.gpsimd.tensor_scalar(zve[:], zmv[:, n, :, 1], LN_EPS, None, ALU.add).then_inc(zpow_step, 1)
                pool.wait_ge(zpow_step, c * 2 + 1)
                nc.gpsimd.tensor_tensor(zrs[:, n, :], zve[:], half_neg[:, 0:NZ], ALU.pow).then_inc(zpow_step, 1)

            deviation(0, 0, True)
            deviation(1, 1, False)
            with pool.Fori(1, NCH // 2) as u:
                for n in range(2):
                    deviation(u * 2 + n, n, False)


def kernel(L0_attn_x, L0_attn_Wq, L0_attn_bq, L0_attn_Wk, L0_attn_bk, L0_attn_Wv, L0_attn_bv, L0_attn_Wo, L0_attn_bo,
           L0_ffn_router_w, L0_ffn_w1, L0_ffn_w2):
    import concourse.bacc as bacc
    from concourse.bass_utils import run_bass_kernel_spmd

    x = np.ascontiguousarray(L0_attn_x)
    w1, w2 = np.asarray(L0_ffn_w1), np.asarray(L0_ffn_w2)

    def tiled(a, k):
        e, _, n = a.shape
        return np.ascontiguousarray(a.reshape(e, k, P, n).transpose(0, 2, 1, 3).reshape(e, P, k * n))

    arrays = {
        "x": x,
        "xT": np.ascontiguousarray(x.reshape(NPAIR, PAIR, KD, P).transpose(0, 3, 2, 1).reshape(NPAIR, P, KD * PAIR)),
        "WqT": np.ascontiguousarray(np.asarray(L0_attn_Wq).T), "bq": np.ascontiguousarray(np.asarray(L0_attn_bq).reshape(KD, P).T),
        "WkT": np.ascontiguousarray(np.asarray(L0_attn_Wk).T), "bk": np.ascontiguousarray(L0_attn_bk),
        "WvT": np.ascontiguousarray(np.asarray(L0_attn_Wv).T), "bv": np.ascontiguousarray(L0_attn_bv),
        "WoT": np.ascontiguousarray(np.asarray(L0_attn_Wo).T), "bo": np.ascontiguousarray(L0_attn_bo),
        "rwT": np.ascontiguousarray(np.asarray(L0_ffn_router_w).T),
        "w1T": tiled(w1.transpose(0, 2, 1), KD), "w2T": tiled(w2.transpose(0, 2, 1), KF),
        "consts": shape_constants(),
    }
    nc = bacc.Bacc("TRN2", target_bir_lowering=False, num_devices=1)
    args = {n: nc.dram_tensor(f"in_{n}", a.shape, F32, kind="ExternalInput").ap() for n, a in arrays.items()}
    out = nc.dram_tensor("out_y", (B, L, D), F32, kind="ExternalOutput").ap()
    build(nc, out=out, **args)
    res = run_bass_kernel_spmd(nc, [{f"in_{n}": a for n, a in arrays.items()}], core_ids=[0])
    return res.results[0]["out_y"]
```
